# Optimizing a Trainium2 kernel written in Bass

```python
import numpy as np
import jax
import jax.numpy as jnp

def _softmax(x, axis=-1):
    return jax.nn.softmax(x, axis=axis)

def _gelu(x):
    return jax.nn.gelu(x, approximate=True)

def _silu(x):
    return jax.nn.silu(x)

def _sigmoid(x):
    return jax.nn.sigmoid(x)

def _layernorm(x, axis=-1, eps=1e-05):
    m = jnp.mean(x, axis=axis, keepdims=True)
    v = jnp.var(x, axis=axis, keepdims=True)
    return (x - m) / jnp.sqrt(v + eps)

def _scatter_add(tgt, idx, src, axis=0):
    return tgt.at[idx].add(src)

def _segment_sum(src, seg, n):
    return jax.ops.segment_sum(src, seg, n)
kernel_name = 'mk_sandwich_d1_jaxref_r8_aa481d'

def setup_inputs(seed: int=0):
    np.random.seed(seed)
    _w = jnp.asarray

    def _L0_attn_setup():
        import jax, jax.numpy as jnp
        import numpy as np
        B, N, C = (2, 256, 128)
        H = 16
        D = C // H
        key = jax.random.key(seed)
        ks = jax.random.split(key, 5)
        s = 0.02
        return {'x': jax.random.normal(ks[0], (B, N, C), dtype=jnp.float32), 'qkv_w': jax.random.normal(ks[1], (C, 3 * C), dtype=jnp.float32) * s, 'qkv_b': jax.random.normal(ks[2], (3 * C,), dtype=jnp.float32) * s, 'proj_w': jax.random.normal(ks[3], (C, C), dtype=jnp.float32) * s, 'proj_b': jax.random.normal(ks[4], (C,), dtype=jnp.float32) * s}
    _L0_attn_in = _L0_attn_setup()

    def _L0_ffn_setup():
        import jax, jax.numpy as jnp
        import numpy as np
        D_IN, D_HID = (128, 512)

        def _ternary(key, shape):
            return jax.random.randint(key, shape, -1, 2).astype(jnp.float32)

        def _tlin(x, w, s):
            return jnp.einsum('bsi,oi->bso', x, w) * s
        key = jax.random.key(seed)
        ks = jax.random.split(key, 12)
        inv = lambda fan: 1.0 / np.sqrt(fan).astype(np.float32)
        return {'x': jax.random.normal(ks[0], (4, 256, D_IN), dtype=jnp.float32), 'w1_w': _ternary(ks[1], (D_HID, D_IN)), 'w1_s': jax.random.uniform(ks[2], (D_HID,), dtype=jnp.float32) * inv(D_IN), 'w2_w': _ternary(ks[3], (D_HID, D_IN)), 'w2_s': jax.random.uniform(ks[4], (D_HID,), dtype=jnp.float32) * inv(D_IN), 'h1_w': _ternary(ks[5], (D_HID, D_HID)), 'h1_s': jax.random.uniform(ks[6], (D_HID,), dtype=jnp.float32) * inv(D_HID), 'h2_w': _ternary(ks[7], (D_HID, D_HID)), 'h2_s': jax.random.uniform(ks[8], (D_HID,), dtype=jnp.float32) * inv(D_HID), 'w3_w': _ternary(ks[9], (D_IN, D_HID)), 'w3_s': jax.random.uniform(ks[10], (D_IN,), dtype=jnp.float32) * inv(D_HID)}
    _L0_ffn_in = _L0_ffn_setup()
    _d = {'L0_attn_x': _L0_attn_in['x'], 'L0_attn_qkv_w': _L0_attn_in['qkv_w'], 'L0_attn_qkv_b': _L0_attn_in['qkv_b'], 'L0_attn_proj_w': _L0_attn_in['proj_w'], 'L0_attn_proj_b': _L0_attn_in['proj_b'], 'L0_ffn_w1_w': _L0_ffn_in['w1_w'], 'L0_ffn_w1_s': _L0_ffn_in['w1_s'], 'L0_ffn_w2_w': _L0_ffn_in['w2_w'], 'L0_ffn_w2_s': _L0_ffn_in['w2_s'], 'L0_ffn_h1_w': _L0_ffn_in['h1_w'], 'L0_ffn_h1_s': _L0_ffn_in['h1_s'], 'L0_ffn_h2_w': _L0_ffn_in['h2_w'], 'L0_ffn_h2_s': _L0_ffn_in['h2_s'], 'L0_ffn_w3_w': _L0_ffn_in['w3_w'], 'L0_ffn_w3_s': _L0_ffn_in['w3_s']}
    _x0 = _d['L0_attn_x']
    _d['L0_attn_x'] = jax.random.normal(jax.random.fold_in(jax.random.key(seed), 1), (16, 512, 128), dtype=_x0.dtype)
    del _x0
    return _d

def reference(L0_attn_x, L0_attn_qkv_w, L0_attn_qkv_b, L0_attn_proj_w, L0_attn_proj_b, L0_ffn_w1_w, L0_ffn_w1_s, L0_ffn_w2_w, L0_ffn_w2_s, L0_ffn_h1_w, L0_ffn_h1_s, L0_ffn_h2_w, L0_ffn_h2_s, L0_ffn_w3_w, L0_ffn_w3_s):

    def _L0_attn_ref(x, qkv_w, qkv_b, proj_w, proj_b):
        import jax, jax.numpy as jnp
        import numpy as np
        B, N, C = (2, 256, 128)
        H = 16
        D = C // H
        b, n, c = x.shape
        scale = (c // H) ** (-0.5)
        qkv = x @ qkv_w + qkv_b
        qkv = qkv.reshape(b, n, 3, H, D)
        q, k, v = jnp.moveaxis(qkv, 2, 0)
        attn = jnp.einsum('bnhd,bmhd->bhnm', q, k) * scale
        attn = jax.nn.softmax(attn, axis=-1)
        out = jnp.einsum('bhnm,bmhd->bnhd', attn, v).reshape(b, n, c)
        out = out @ proj_w + proj_b
        return out

    def _L0_ffn_ref(x, w1_w, w1_s, w2_w, w2_s, h1_w, h1_s, h2_w, h2_s, w3_w, w3_s):
        import jax, jax.numpy as jnp
        import numpy as np
        D_IN, D_HID = (128, 512)

        def _ternary(key, shape):
            return jax.random.randint(key, shape, -1, 2).astype(jnp.float32)

        def _tlin(x, w, s):
            return jnp.einsum('bsi,oi->bso', x, w) * s
        h = jax.nn.silu(_tlin(x, w1_w, w1_s)) * _tlin(x, w2_w, w2_s)
        h = jax.nn.gelu(_tlin(h, h1_w, h1_s), approximate=False)
        h = jax.nn.gelu(_tlin(h, h2_w, h2_s), approximate=False)
        return _tlin(h, w3_w, w3_s)
    x = L0_attn_x
    x = x + _layernorm(_L0_attn_ref(_layernorm(x, axis=-1), L0_attn_qkv_w, L0_attn_qkv_b, L0_attn_proj_w, L0_attn_proj_b), axis=-1)
    x = x + _layernorm(_L0_ffn_ref(_layernorm(x, axis=-1), L0_ffn_w1_w, L0_ffn_w1_s, L0_ffn_w2_w, L0_ffn_w2_s, L0_ffn_h1_w, L0_ffn_h1_s, L0_ffn_h2_w, L0_ffn_h2_s, L0_ffn_w3_w, L0_ffn_w3_s), axis=-1)
    return x

_drawn_inputs = setup_inputs


def setup_inputs(seed=0):
    import zlib

    import numpy as np

    out = dict(_drawn_inputs(seed))
    spreads = {}
    factors = {}
    for name, (base, spread) in spreads.items():
        noise = np.random.default_rng([zlib.crc32(name.encode()), seed]).standard_normal(out[name].shape)
        drawn = base * np.exp(spread * noise) if base else spread * noise
        out[name] = jnp.asarray(drawn.astype(out[name].dtype))
    for name, factor in factors.items():
        out[name] = (out[name] * factor).astype(out[name].dtype)
    return out
```

```python
import concourse.bass as bass
from concourse import mybir
from contextlib import ExitStack


F32 = mybir.dt.float32
F32R = mybir.dt.float32r
ALU = mybir.AluOpType
ACT = mybir.ActivationFunctionType
AX = mybir.AxisListType

B, N, C, H = 16, 512, 128, 16
D = C // H
P = 128
NT = N // P
G = H // 4
HID = 512
HC = HID // P
QROWS = 3 * 4 * D
MROWS = 8
QUARTERS = 4 * G
LEAD = 6
SCALE = float(D) ** -0.5
EPS = 1e-5
LN_IN, LN_POST, LN_MID, LN_OUT = range(4)

FILLS = (
    [("w3T", -3, "dve", 0), ("h2_0", -2, "act", 1), ("xT", 1, "act", 0), ("h2_1", -2, "act", 1), ("q", 1, "act", 0),
     ("max1", 0, "act", 0), ("h2_2", -2, "act", 1), ("proj", -1, "act", 0), ("h2_3", -2, "act", 1),
     ("projT", -1, "dve", 0), ("k", 1, "act", 0), ("v", 1, "dve", 1), ("max2", 0, "act", 1), ("x2T", -1, "act", 0)]
    + [(f"{n}{o}", -1, e, bank) for o in range(HC) for n, e, bank in (("gate", "act", 1), ("up", "dve", 0))]
    + [("max3", 0, "act", 0), ("h1_0", -1, "act", 1), ("h1_1", -1, "act", 1), ("h1_2", -1, "act", 1),
       ("max0", 1, "act", 0), ("h1_3", -1, "act", 1), ("w3", -2, "act", 0)]
)
ORDER = [f[0] for f in FILLS]
STEADY = 4


def valid(j):
    return not isinstance(j, int) or 0 <= j < B


def fills_before(b, engine=None):
    if isinstance(b, int):
        return sum(valid(c + off) for c in range(-1, b) for _, off, e, _ in FILLS if engine in (None, e))
    each = sum(engine in (None, e) for _, _, e, _ in FILLS)
    return b * each + (fills_before(STEADY, engine) - STEADY * each)


def fill_count(b, name, engine=None):
    upto = FILLS[:ORDER.index(name) + 1]
    return fills_before(b, engine) + sum(valid(b + off) for _, off, e, _ in upto if engine in (None, e))


def bank_of(name):
    return FILLS[ORDER.index(name)][3]


def fill_engine(name):
    return FILLS[ORDER.index(name)][2]


def bank_user_before(b, name):
    at = ORDER.index(name)
    for n, off, _, _ in reversed(FILLS[:at]):
        if bank_of(n) == bank_of(name) and valid(b + off):
            return b, n
    if isinstance(b, int) and b <= -1:
        return None
    for n, off, _, _ in reversed(FILLS):
        if bank_of(n) == bank_of(name) and valid(b - 1 + off):
            return b - 1, n
    return None


def wait(eng, sem, value):
    if not isinstance(value, int) or value > 0:
        eng.wait_ge(sem, value)


def build(nc, x, qkv_w, qkv_b, proj_w, proj_b, w1_w, w1_s, w2_w, w2_s, h1_w, h1_s, h2_w, h2_s, w3_w, w3_s, out):
    ctx = ExitStack()
    with ctx:
        def sb(name, shape, dt=F32):
            return ctx.enter_context(nc.sbuf_tensor(name, shape, dt))

        def sem(name):
            return ctx.enter_context(nc.semaphore(name))

        ident = sb("ident", [P, P])
        k_rows = sb("k_rows", [P, H, N], F32R)
        q_rows = sb("q_rows", [P, G, N], F32R)
        probs = sb("probs", [P, 2, 4, N])
        ones_row = probs[0:1, 0, :, :]
        v_cols = sb("v_cols", [P, NT, H, 2 * D])
        hid_a = sb("hid_a", [P, 2, HC, N], F32R)
        hid_b = sb("hid_b", [P, 2, HC, N], F32R)
        pre = sb("pre", [P, HC, N])
        gated = sb("gated", [P, HC, N])
        acts = sb("acts", [P, HC, N])
        w1T = sb("w1T", [P, 2, 1, HID], F32R)
        w2T = sb("w2T", [P, 2, 1, HID], F32R)
        h1T = sb("h1T", [P, 2, HC, HID], F32R)
        h2T = sb("h2T", [P, 2, HC, HID], F32R)
        w3T = sb("w3T", [P, 2, 1, HID], F32R)
        qkvp = sb("qkvp", [P, 2, 4 * C], F32R)
        qk_bias = sb("qk_bias", [P, 2])
        v_bias = sb("v_bias", [P, C])
        proj_bias = sb("proj_bias", [P, 1])
        s1 = sb("s1", [P, HC])
        s2 = sb("s2", [P, HC])
        s2_half = sb("s2_half", [P, HC])
        sh1 = sb("sh1", [P, HC])
        sh2 = sb("sh2", [P, HC])
        s3 = sb("s3", [P, 1])
        x_in = sb("x_in", [P, NT, C])
        x_res = sb("x_res", [P, NT, C])
        x_mid = sb("x_mid", [P, NT, C])
        x_kept = sb("x_kept", [P, NT, C])
        y_out = sb("y_out", [P, NT, C])
        turned = sb("turned", [P, N])
        xT = sb("xT", [P, 2, N], F32R)
        x2T = xT
        q_split = sb("q_split", [P, 3, N], F32R)
        k_split = sb("k_split", [P, 3, N], F32R)
        v_tok = sb("v_tok", [P, NT, C])
        maxes = sb("maxes", [P, 2, NT, 4])
        max_split = sb("max_split", [P, 2, NT, MROWS])
        o_group = sb("o_group", [P, N])
        o_chan = sb("o_chan", [P, 2, N])
        oT = sb("oT", [P, 2, N], F32R)
        y_post = o_chan[:, 0, :].rearrange("p (k c) -> p k c", c=C)
        mid_norm = y_post
        proj_out = o_chan[:, 1, :]
        ffn_out = turned
        stats = [sb(f"stats{n}", [P, NT, 6]) for n in range(4)]
        mean_var = [sb(f"mean_var{n}", [P, NT, 2]) for n in range(4)]
        rstd = [sb(f"rstd{n}", [P, NT]) for n in range(4)]
        minus_half = sb("minus_half", [P, NT])

        sT_ps = ctx.enter_context(nc.psum_tensor("sT_ps", [P, 3, N], F32))
        s_ps = ctx.enter_context(nc.psum_tensor("s_ps", [P, 2, N], F32))
        o_ps = ctx.enter_context(nc.psum_tensor("o_ps", [P, N], F32))
        fill_ps = ctx.enter_context(nc.psum_tensor("fill_ps", [P, 2, N], F32))

        rows_loaded = sem("rows_loaded")
        small_loaded = sem("small_loaded")
        ones_placed = sem("ones_placed")
        consts_pool = sem("consts_pool")
        zeros_dve = sem("zeros_dve")
        wT_turned = sem("wT_turned")
        halved = sem("halved")
        w_hi = sem("w_hi")
        w_lo = sem("w_lo")
        x_in_loaded = sem("x_in_loaded")
        x_res_loaded = sem("x_res_loaded")
        kq_moved = [sem(f"kq_moved{g}") for g in range(G)]
        o_moved = sem("o_moved")
        out_stored = sem("out_stored")
        sT_done = sem("sT_done")
        s_done = sem("s_done")
        pv_done = sem("pv_done")
        fill_done = sem("fill_done")
        exp_done = sem("exp_done")
        emptied = {"act": sem("emptied_act"), "dve": sem("emptied_dve")}
        tanh_done = sem("tanh_done")
        gelu_done = sem("gelu_done")
        max_done = sem("max_done")
        max_hi_done = sem("max_hi_done")
        max_split_done = sem("max_split_done")
        o_emptied = sem("o_emptied")
        stats_done = [sem(f"stats_done{n}") for n in range(4)]
        mean_done = [sem(f"mean_done{n}") for n in range(4)]
        eps_added = [sem(f"eps_added{n}") for n in range(4)]
        rstd_done = [sem(f"rstd_done{n}") for n in range(4)]
        normed = [sem(f"normed{n}") for n in range(4)]
        sums_inverted = sem("sums_inverted")
        o_scaled = sem("o_scaled")
        o_hi_done = sem("o_hi_done")
        oT_split = sem("oT_split")
        x_hi_done = sem("x_hi_done")
        xT_split = sem("xT_split")
        x2_hi_done = sem("x2_hi_done")
        x2T_split = sem("x2T_split")
        q_hi_done = sem("q_hi_done")
        q_split_done = sem("q_split_done")
        k_hi_done = sem("k_hi_done")
        k_split_done = sem("k_split_done")
        v_placed = sem("v_placed")
        x_mid_done = sem("x_mid_done")
        x_mid_kept = sem("x_mid_kept")
        out_added = sem("out_added")
        silu_done = sem("silu_done")
        hid_hi_done = sem("hid_hi_done")
        last_hi_done = sem("last_hi_done")
        hid_lo_dve = sem("hid_lo_dve")
        hid_lo_pool = sem("hid_lo_pool")

        xr = x.rearrange("b (k p) c -> b p k c", p=P)
        outr = out.rearrange("b (k p) c -> b p k c", p=P)

        def turned_weights():
            yield [pre[:, 0, P * o:P * o + P] for o in range(HC)], w1T, 0
            yield [pre[:, 1, P * o:P * o + P] for o in range(HC)], w2T, 0
            yield [pre[:, 2, P * k:P * k + P] for k in range(HC)], w3T, 0
            for src, dst in ((gated, h1T), (acts, h2T)):
                for k in range(HC):
                    yield [src[:, o, P * k:P * k + P] for o in range(HC)], dst, k

        TURNED = 3 + 2 * HC
        block = ctx.enter_context(nc.Block())

        counted = {eng.engine: [eng.alloc_register(f"counted{n}") for n in range(1 + G)]
                   for eng in (nc.sync, nc.vector, nc.gpsimd)}

        def wait_apart(eng, *counts):
            ready = []
            for n, (q, v) in enumerate(counts):
                if not isinstance(v, int):
                    eng.reg_mov(counted[eng.engine][n], v)
                    v = counted[eng.engine][n]
                ready.append((q, v))
            eng.wait_ge(consts_pool, 6)
            for q, v in ready:
                wait(eng, q, v)

        def iterations(eng, body):
            for b in range(-1, STEADY):
                body(b)
            with eng.Fori(STEADY, B - 2) as b:
                body(b)
            for b in range(B - 2, B + 3):
                body(b)

        def score_tile(b, t):
            s = t + LEAD
            j = b + s // QUARTERS
            return j, s % QUARTERS // 4, s % 4

        @block.sync
        def _(sp):
            sp.dma_start(x_in[:], xr[0]).then_inc(x_in_loaded, 16)
            sp.dma_start(pre[:, 3, :384], qkv_w).then_inc(rows_loaded, 16)
            sp.dma_start(pre[:, 3, 384:], proj_w).then_inc(rows_loaded, 16)
            sp.dma_start(pre[:, 0, :].rearrange("p (o i) -> p o i", i=C), w1_w.rearrange("(o p) i -> p o i", p=P)).then_inc(rows_loaded, 16)
            sp.dma_start(pre[:, 1, :].rearrange("p (o i) -> p o i", i=C), w2_w.rearrange("(o p) i -> p o i", p=P)).then_inc(rows_loaded, 16)
            sp.dma_start(pre[:, 2, :], w3_w).then_inc(rows_loaded, 16)
            sp.dma_start(gated[:], h1_w.rearrange("(o p) i -> p o i", p=P)).then_inc(rows_loaded, 16)
            sp.dma_start(acts[:], h2_w.rearrange("(o p) i -> p o i", p=P)).then_inc(rows_loaded, 16)
            sp.dma_start(qk_bias[:], qkv_b[0:2 * C].rearrange("(a p) -> p a", p=P), allow_slow_non_contiguous=True).then_inc(small_loaded, 16)
            sp.dma_start(v_bias[:], qkv_b[2 * C:3 * C].rearrange("(a c) -> a c", a=1).broadcast_to([P, C])).then_inc(small_loaded, 16)
            sp.dma_start(proj_bias[:], proj_b.rearrange("(a p) -> p a", p=P), allow_slow_non_contiguous=True).then_inc(small_loaded, 16)
            for dst, src in ((s1, w1_s), (s2, w2_s), (sh1, h1_s), (sh2, h2_s), (s3, w3_s)):
                sp.dma_start(dst[:], src.rearrange("(a p) -> p a", p=P), allow_slow_non_contiguous=True).then_inc(small_loaded, 16)
            sp.wait_ge(consts_pool, 6)
            sp.wait_ge(zeros_dve, 1)
            for i in range(4):
                for row in (QROWS + i, QROWS + 4 + i):
                    sp.dma_start(k_rows[row:row + 1].rearrange("p (g i) n -> p g i n", i=4)[:, :, i, :].bitcast(F32),
                                 ones_row).then_inc(ones_placed, 16)

            def move_kq(j, g):
                if not valid(j):
                    return
                wait_apart(sp, (k_split_done, j + 1), (sT_done, (j - 1) * 64 + 16 * g + 16))
                sp.dma_start(q_rows[0:QROWS, g, :].bitcast(F32), q_split[32 * g:32 * g + 32].bitcast(F32)).then_inc(kq_moved[g], 16)
                for i in range(4):
                    h = 4 * g + i
                    sp.dma_start(k_rows[24 * i:24 * i + 24, h, :].bitcast(F32), k_split[D * h:D * h + D].bitcast(F32)).then_inc(kq_moved[g], 16)

            def move_o(j, g):
                if not valid(j):
                    return
                wait_apart(sp, (o_emptied, 4 * j + g + 1), (o_scaled, j),
                           *([(emptied["act"], fill_count(j, "x2T", "act"))] if valid(j - 1) else []))
                for i in range(4):
                    h = 4 * g + i
                    sp.dma_start(o_chan[D * h:D * h + D], o_group[32 * i:32 * i + 2 * D, :]).then_inc(o_moved, 16)

            def body(b):
                move_kq(b, 3)
                move_o(b - 1, 3)
                if valid(b + 2) and (not isinstance(b, int) or b + 2 >= 1):
                    wait_apart(sp, (emptied["act"], fill_count(b, "xT", "act")))
                    sp.dma_start(x_in[:], xr[b + 2]).then_inc(x_in_loaded, 16)
                if valid(b):
                    wait_apart(sp, (x_mid_done, b))
                    sp.dma_start(x_res[:], xr[b]).then_inc(x_res_loaded, 16)
                if valid(b - 3):
                    wait_apart(sp, (out_added, b - 2))
                    sp.dma_start(outr[b - 3], y_out[:]).then_inc(out_stored, 16)
                move_o(b, 0)
                move_kq(b + 1, 0)
                for g in (1, 2):
                    move_kq(b + 1, g)
                    move_o(b, g)

            iterations(sp, body)
            sp.wait_ge(out_stored, 16 * B)

        @block.tensor
        def _(pe):
            pe.wait_ge(consts_pool, 5)
            for n, (blocks, _, _) in enumerate(turned_weights()):
                wait(pe, rows_loaded, 16 * 7)
                if n >= 2:
                    pe.wait_ge(w_lo, n)
                for c, src in enumerate(blocks):
                    last = nc.tensor.transpose(fill_ps[:, n % 2, P * c:P * c + P], src, ident[:])
                last.then_inc(wT_turned, 1)
            pe.wait_ge(w_lo, TURNED + 1)
            pe.wait_ge(ones_placed, 16 * 8)
            pe.wait_ge(zeros_dve, 2)

            def begin(b, name):
                before = bank_user_before(b, name)
                if before:
                    e = fill_engine(before[1])
                    wait(pe, emptied[e], fill_count(*before, e))
                return fill_ps[:, bank_of(name), :]

            def split_product(bank, pairs, part=(0, 1)):
                terms = [(w, xs, u, v) for w, xs in pairs for u, v in ((0, 0), (1, 0), (0, 1))]
                n = len(terms)
                for a in range(part[0] * n // part[1], (part[0] + 1) * n // part[1]):
                    w, xs, u, v = terms[a]
                    last = nc.tensor.matmul(bank, w(u), xs(v), start=(a == 0), stop=(a == n - 1))
                return last

            def hidden(b, name, w, src, step):
                o, part = step // 4, step % 4
                name = f"{name}_{o}"
                bank = begin(b, name) if part == 0 else fill_ps[:, bank_of(name), :]
                last = split_product(bank, [(lambda u, k=k: w[:, u, k, P * o:P * o + P], lambda v, k=k: src[:, v, k, :])
                                            for k in range(HC)], (part, 4))
                if part == 3:
                    last.then_inc(fill_done, 1)

            def turn(b, name, src):
                bank = begin(b, name)
                for k in range(NT):
                    last = nc.tensor.transpose(bank[:, P * k:P * k + P], src(k), ident[:])
                last.then_inc(fill_done, 1)

            def fill(b, u):
                if u == 2 and valid(b - 3):
                    wait(pe, emptied["act"], fill_count(b - 1, "w3", "act"))
                    turn(b, "w3T", lambda k: ffn_out[:, P * k:P * k + P])
                if u == 5 and valid(b + 1):
                    wait(pe, normed[LN_IN], 4 * (b + 2))
                    turn(b, "xT", lambda k: x_in[:, k, :])
                if u in (9, 18) and valid(b + 1):
                    wait(pe, xT_split, b + 2)
                    a = u // 18
                    split_product(begin(b, "qk"[a]), [(lambda u: qkvp[:, u, C * a:C * a + C], lambda v: xT[:, v, :])]).then_inc(fill_done, 1)
                if u == 14 and valid(b - 1):
                    wait(pe, oT_split, b)
                    split_product(begin(b, "proj"), [(lambda u: qkvp[:, u, 3 * C:4 * C], lambda v: oT[:, v, :])]).then_inc(fill_done, 1)
                if u == 16 and valid(b - 1):
                    wait(pe, emptied["act"], fill_count(b, "proj", "act"))
                    turn(b, "projT", lambda k: proj_out[:, P * k:P * k + P])
                if 16 <= u < 20 and valid(b + 1):
                    k = u - 16
                    bank = begin(b, "v") if k == 0 else fill_ps[:, bank_of("v"), :]
                    last = split_product(bank[:, P * k:P * k + P],
                                         [(lambda u: xT[:, u, P * k:P * k + P], lambda v: qkvp[:, v, 2 * C:3 * C])])
                    if k == NT - 1:
                        last.then_inc(fill_done, 1)
                g = u // 16 + 1
                if u % 16 == 10 and valid(b + g // 4):
                    wait(pe, max_split_done, 4 * b + g + 1)
                    bank = begin(b, f"max{g % 4}")
                    for k in range(NT):
                        last = nc.tensor.transpose(bank[0:MROWS, P * k:P * k + P], max_split[:, g % 2, k, :], ident[:])
                    last.then_inc(fill_done, 1)
                if u == 29 and valid(b - 1):
                    wait(pe, normed[LN_MID], 4 * b)
                    turn(b, "x2T", lambda k: mid_norm[:, k, :])
                if 33 <= u < 41 and valid(b - 1):
                    o = (u - 33) // 2
                    wait(pe, x2T_split, b)
                    name, w = (("up", w2T), ("gate", w1T))[u % 2]
                    split_product(begin(b, f"{name}{o}"), [(lambda u: w[:, u, 0, P * o:P * o + P], lambda v: x2T[:, v, :])]).then_inc(fill_done, 1)
                if u < 16 and valid(b - 2):
                    if u == 0:
                        wait(pe, hid_lo_dve, b - 1)
                    if u == 1:
                        wait(pe, hid_lo_pool, 7 * (b - 2) + 5)
                    hidden(b, "h2", h2T, hid_a, u)
                if 44 <= u < 60 and valid(b - 1):
                    if u == 44:
                        wait(pe, hid_lo_pool, 7 * (b - 1) + 4)
                    hidden(b, "h1", h1T, hid_a, u - 44)
                if u >= 60 and valid(b - 2):
                    if u == 60:
                        wait(pe, hid_lo_pool, 7 * (b - 1))
                        begin(b, "w3")
                    last = split_product(fill_ps[:, bank_of("w3"), :], [(lambda u, k=k: w3T[:, u, 0, P * k:P * k + P],
                                                                         lambda v, k=k: hid_b[:, v, k, :]) for k in range(HC)],
                                         (u - 60, 4))
                    if u == 63:
                        last.then_inc(fill_done, 1)

            def transposed_scores(b, t, i):
                g, kt, h, n = t // 4, t % 4, t // 4 * 4 + i, 64 * b + 4 * t + i
                if kt == 0 and i == 0:
                    at = (b - 1, "max0") if g == 0 else (b, f"max{g}")
                    wait(pe, emptied["act"], fill_count(*at, "act"))
                u = 4 * t + i
                wait(pe, exp_done, n if u == 0 else n - 3 if u < 3 else n - 2)
                nc.tensor.matmul(sT_ps[:, u % 3, :], k_rows[0:QROWS + MROWS, h, P * kt:P * kt + P],
                                 q_rows[0:QROWS + MROWS, g, :], start=True, stop=True).then_inc(sT_done, 1)

            def scores(b, t, i):
                j, g, qt = score_tile(b, t)
                if not valid(j):
                    return
                if qt == 0 and i == 0:
                    wait(pe, kq_moved[g], 80 * (j + 1))
                wait(pe, max_done, 64 * j + 16 * g + 4 * qt + i - 1)
                nc.tensor.matmul(s_ps[:, i % 2, :], q_rows[0:QROWS, g, P * qt:P * qt + P],
                                 k_rows[0:QROWS, 4 * g + i, :], start=True, stop=True).then_inc(s_done, 1)

            def outputs(j, t):
                if not valid(j):
                    return
                g, kt = t // 4, t % 4
                if kt == 0:
                    wait(pe, o_emptied, 4 * j + g)
                    wait(pe, v_placed, 4 * j + g + 1)
                wait(pe, exp_done, 64 * j + 4 * t + 4)
                for i in range(4):
                    last = nc.tensor.matmul(o_ps[32 * i:32 * i + 2 * D, :], v_cols[:, kt, 4 * g + i, :], probs[:, t % 2, i, :],
                                            start=(kt == 0), stop=(kt == 3))
                last.then_inc(pv_done, 1)

            def body(b):
                for t in range(QUARTERS):
                    for i in range(4):
                        if valid(b):
                            transposed_scores(b, t, i)
                        scores(b, t, i)
                        fill(b, 4 * t + i)
                    outputs(b - 1 if t == 0 else b, (t - 1) % QUARTERS)

            iterations(pe, body)

        @block.scalar
        def _(act):
            act.wait_ge(small_loaded, 16 * 8)

            def empty(b, name, dst, src=None, rows=P, **kw):
                act.wait_ge(fill_done, fill_count(b, name))
                src = fill_ps[0:rows, bank_of(name), :]
                nc.scalar.activation(dst, src, ACT.Identity, **kw).then_inc(emptied["act"], 1)

            def gelu(last):
                act.wait_ge(emptied["act"], last)
                for half in (slice(0, 2), slice(2, 4)):
                    nc.scalar.activation(acts[:, half, :], pre[:, half, :], ACT.Gelu).then_inc(gelu_done, 1)

            def empty_maxima(b, g):
                empty(b, f"max{g}", q_rows[QROWS:QROWS + MROWS, g, :], rows=MROWS)

            def other(b, u):
                if u in (3, 7, 11, 15) and valid(b - 2):
                    o = u // 4
                    empty(b, f"h2_{o}", pre[:, o, :], scale=sh2[:, o:o + 1])
                if u == 5 and valid(b + 1):
                    wait(act, x2T_split, b - 1)
                    empty(b, "xT", turned[:])
                if u == 9 and valid(b + 1):
                    wait(act, xT_split, b + 2)
                    empty(b, "q", turned[:], bias=qk_bias[:, 0:1])
                if u == 14 and valid(b - 1):
                    empty(b, "proj", proj_out[:], bias=proj_bias[:, 0:1])
                if u == 16 and valid(b - 2):
                    gelu(fill_count(b, "h2_3", "act"))
                if u == 18 and valid(b + 1):
                    wait(act, q_split_done, b + 2)
                    empty(b, "k", turned[:], bias=qk_bias[:, 1:2])
                if u == 20 and valid(b - 2):
                    wait(act, x_mid_done, b - 1)
                    wait(act, out_added, b - 2)
                    nc.scalar.activation(x_kept[:], x_mid[:], ACT.Identity).then_inc(x_mid_kept, 1)
                if 21 <= u < 25 and valid(b - 2):
                    if u % 2:
                        wait(act, gelu_done, 4 * (b - 2) + 3 + (u - 21) // 2)
                    nc.scalar.activation(hid_b[:, 0, u - 21, :], acts[:, u - 21, :], ACT.Identity).then_inc(last_hi_done, 1)
                g = u // 16 + 1
                if u % 16 == 10 and valid(b + g // 4):
                    empty_maxima(b, g % 4)
                if u == 29 and valid(b - 1):
                    wait(act, k_split_done, min(b + 2, B) if isinstance(b, int) else b + 2)
                    empty(b, "x2T", turned[:])
                if 33 <= u < 41 and valid(b - 1):
                    o = (u - 33) // 2
                    if u % 2:
                        empty(b, f"gate{o}", pre[:, o, :], scale=s1[:, o:o + 1])
                    else:
                        act.wait_ge(emptied["act"], fill_count(b, f"gate{o}", "act"))
                        nc.scalar.activation(acts[:, o, :], pre[:, o, :], ACT.Tanh, scale=0.5).then_inc(tanh_done, 1)
                if u in (47, 51, 55, 59) and valid(b - 1):
                    o = (u - 47) // 4
                    empty(b, f"h1_{o}", pre[:, o, :], scale=sh1[:, o:o + 1])
                if u == 60 and valid(b - 1):
                    gelu(fill_count(b, "h1_3", "act"))
                if u == 63 and valid(b - 2):
                    wait(act, x2T_split, min(b, B) if isinstance(b, int) else b)
                    empty(b, "w3", ffn_out[:], scale=s3[:, 0:1])

            def body(b):
                for t in range(QUARTERS):
                    for i in range(4):
                        u = 4 * t + i
                        if valid(b):
                            if i == 0:
                                wait(act, pv_done, 16 * b + t - 1)
                            act.wait_ge(sT_done, 64 * b + u + 1)
                            nc.scalar.activation(probs[:, t % 2, i, :], sT_ps[:, u % 3, :], ACT.Exp,
                                                 scale=SCALE).then_inc(exp_done, 1)
                        other(b, u)

            iterations(act, body)

        @block.vector
        def _(dve):
            nc.vector.memset(k_rows[:, 0:H // 2, :].bitcast(F32), 0.0).then_inc(zeros_dve, 1)
            nc.vector.memset(o_ps[:], 0.0).then_inc(zeros_dve, 1)
            dve.wait_ge(rows_loaded, 16 * 7)
            nc.vector.tensor_copy(qkvp[:, 0, :], pre[:, 3, :]).then_inc(w_hi, 1)
            dve.wait_ge(w_hi, 1)
            nc.vector.tensor_tensor(qkvp[:, 1, :], pre[:, 3, :], qkvp[:, 0, :].bitcast(F32), ALU.subtract).then_inc(w_lo, 1)
            for n, (_, dst, k) in enumerate(turned_weights()):
                dve.wait_ge(wT_turned, n + 1)
                nc.vector.tensor_copy(dst[:, 0, k, :], fill_ps[:, n % 2, :]).then_inc(w_hi, 1)
                dve.wait_ge(w_hi, n + 2)
                nc.vector.tensor_tensor(dst[:, 1, k, :], fill_ps[:, n % 2, :], dst[:, 0, k, :].bitcast(F32), ALU.subtract).then_inc(w_lo, 1)
            dve.wait_ge(small_loaded, 16 * 8)
            nc.vector.tensor_scalar(s2_half[:], s2[:], 0.5, None, ALU.mult).then_inc(halved, 1)
            dve.wait_ge(halved, 1)

            def take_stats(ln, src, tiles=range(NT)):
                for k in tiles:
                    nc.vector.bn_stats(stats[ln][:, k, :], src[:, k, :]).then_inc(stats_done[ln], 1)

            def aggregate(ln, j):
                wait_apart(dve, (stats_done[ln], 4 * (j + 1)))
                for k in range(NT):
                    nc.vector.bn_aggr(mean_var[ln][:, k, :], stats[ln][:, k, :]).then_inc(mean_done[ln], 1)

            def normalise(ln, j, dst, src, tiles=range(NT)):
                dve.wait_ge(rstd_done[ln], j + 1)
                for k in tiles:
                    nc.vector.tensor_scalar(dst[:, k, :], src[:, k, :], mean_var[ln][:, k, 0:1], rstd[ln][:, k:k + 1],
                                            ALU.subtract, ALU.mult).then_inc(normed[ln], 1)

            def tokens(a):
                return a[:].rearrange("p (k c) -> p k c", c=C)

            def twice(a):
                return a[:].rearrange("p (a n) -> p a n", a=1).broadcast_to([P, 2, N])

            def empty_o(j, g):
                if not valid(j):
                    return
                dve.wait_ge(pv_done, 16 * j + 4 * g + 4)
                wait(dve, o_moved, 64 * (4 * j + g))
                nc.vector.tensor_copy(o_group[:], o_ps[:]).then_inc(o_emptied, 1)

            def split_hi(dst, src, part):
                nc.vector.tensor_copy(dst[:, 0, part, :], src[:, part, :]).then_inc(hid_hi_done, 1)

            def split_lo(dst, src, part):
                nc.vector.tensor_tensor(dst[:, 1, part, :], src[:, part, :], dst[:, 0, part, :].bitcast(F32), ALU.subtract).then_inc(hid_lo_dve, 1)

            def other(b, u):
                if u == 3 and valid(b - 3):
                    dve.wait_ge(fill_done, fill_count(b, "w3T"))
                    wait(dve, out_stored, 16 * (b - 3))
                    nc.vector.tensor_copy(y_out[:], tokens_of_bank("w3T")).then_inc(emptied["dve"], 1)
                if u % 16 == 4:
                    empty_o(b - 1 if u == 4 else b, (u // 16 - 1) % 4)
                if u in (5, 6) and valid(b - 3):
                    dve.wait_ge(emptied["dve"], fill_count(b, "w3T", "dve"))
                    take_stats(LN_OUT, y_out, range(2 * u - 10, 2 * u - 8))
                if u == 6 and valid(b + 1):
                    wait_apart(dve, (emptied["act"], fill_count(b, "xT", "act")))
                    nc.vector.tensor_copy(xT[:, 0, :], turned[:]).then_inc(x_hi_done, 1)
                if u == 7 and valid(b - 3):
                    aggregate(LN_OUT, b - 3)
                if 8 <= u < 12 and valid(b - 1):
                    dve.wait_ge(o_moved, 256 * b)
                    part = slice(P * (u - 8), P * (u - 7))
                    nc.vector.reciprocal(o_chan[:, 1, part], o_chan[:, 1, part]).then_inc(sums_inverted, 1)
                if u == 12 and valid(b - 1):
                    dve.wait_ge(sums_inverted, 4 * b)
                    nc.vector.tensor_tensor(o_chan[:, 0, :], o_chan[:, 0, :], o_chan[:, 1, :], ALU.mult).then_inc(o_scaled, 1)
                    wait_apart(dve, (o_scaled, b), (oT_split, b - 1))
                    nc.vector.tensor_copy(oT[:, 0, :], o_chan[:, 0, :]).then_inc(o_hi_done, 1)
                if u in (13, 14) and valid(b - 3):
                    normalise(LN_OUT, b - 3, y_out, y_out, range(2 * u - 26, 2 * u - 24))
                if u == 15 and valid(b + 1):
                    wait_apart(dve, (emptied["act"], fill_count(b, "q", "act")),
                               *((kq_moved[g], 80 * (b + 1)) for g in range(G)))
                    nc.vector.tensor_copy(q_split[:, 0:2, :], twice(turned)).then_inc(q_hi_done, 1)
                if u == 17 and valid(b - 1):
                    dve.wait_ge(fill_done, fill_count(b, "projT"))
                    nc.vector.tensor_copy(y_post[:], tokens_of_bank("projT")).then_inc(emptied["dve"], 1)
                if u == 18 and valid(b - 1):
                    dve.wait_ge(emptied["dve"], fill_count(b, "projT", "dve"))
                    take_stats(LN_POST, y_post)
                if u == 19 and valid(b - 1):
                    aggregate(LN_POST, b - 1)
                if u == 21 and valid(b + 1):
                    dve.wait_ge(fill_done, fill_count(b, "v"))
                    wait(dve, v_placed, 4 * (b + 1))
                    nc.vector.tensor_copy(v_tok[:], tokens_of_bank("v")).then_inc(emptied["dve"], 1)
                if u == 22 and valid(b - 1):
                    normalise(LN_POST, b - 1, y_post, y_post)
                if u == 23 and valid(b + 1):
                    wait_apart(dve, (emptied["act"], fill_count(b, "k", "act")))
                    nc.vector.tensor_copy(k_split[:, 0:3:2, :], twice(turned)).then_inc(k_hi_done, 1)
                if u == 25 and valid(b - 1):
                    dve.wait_ge(x_mid_done, b)
                    take_stats(LN_MID, x_mid)
                if u == 26 and valid(b - 1):
                    aggregate(LN_MID, b - 1)
                if u == 28 and valid(b - 1):
                    normalise(LN_MID, b - 1, mid_norm, x_mid)
                if u == 30 and valid(b - 1):
                    wait_apart(dve, (emptied["act"], fill_count(b, "x2T", "act")))
                    nc.vector.tensor_copy(x2T[:, 0, :], turned[:]).then_inc(x2_hi_done, 1)
                if valid(b - 1) and 34 <= u <= 40 and u % 2 == 0:
                    o = (u - 34) // 2
                    dve.wait_ge(fill_done, fill_count(b, f"up{o}"))
                    dve.wait_ge(emptied["act"], fill_count(b, f"gate{o}", "act"))
                    nc.vector.scalar_tensor_tensor(out=gated[:, o, :], in0=fill_ps[:, bank_of(f"up{o}"), :], scalar=s2_half[:, o:o + 1],
                                                   in1=pre[:, o, :], op0=ALU.mult, op1=ALU.mult).then_inc(emptied["dve"], 1)
                if valid(b - 1) and 35 <= u <= 41 and u % 2:
                    o = (u - 35) // 2
                    wait(dve, tanh_done, 4 * (b - 1) + o + 1)
                    wait(dve, emptied["dve"], fill_count(b, f"up{o}", "dve"))
                    nc.vector.scalar_tensor_tensor(out=gated[:, o, :], in0=acts[:, o, :], scalar=1.0, in1=gated[:, o, :], op0=ALU.add,
                                                   op1=ALU.mult).then_inc(silu_done, 1)
                if valid(b - 1) and 36 <= u <= 42 and u % 2 == 0:
                    o = (u - 36) // 2
                    wait_apart(dve, (silu_done, 4 * (b - 1) + o + 1))
                    split_hi(hid_a, gated, slice(o, o + 1))
                if u in (46, 47) and valid(b + 2):
                    dve.wait_ge(x_in_loaded, 16 * (b + 3))
                    take_stats(LN_IN, x_in, range(2 * u - 92, 2 * u - 90))
                if u == 48 and valid(b + 2):
                    aggregate(LN_IN, b + 2)
                if u in (52, 53) and valid(b + 2):
                    normalise(LN_IN, b + 2, x_in, x_in, range(2 * u - 104, 2 * u - 102))
                if u in (62, 63) and valid(b - 1):
                    wait_apart(dve, (gelu_done, 4 * (b - 1) + u - 61))
                    split_hi(hid_a, acts, slice(2 * u - 124, 2 * u - 122))
                if u == 63 and valid(b - 1):
                    dve.wait_ge(hid_hi_done, 6 * (b - 1) + 5)
                    split_lo(hid_a, acts, slice(0, 2))

            def tokens_of_bank(name):
                return fill_ps[:, bank_of(name), :].rearrange("p (k c) -> p k c", c=C)

            def maximum(b, t, i):
                j, g, qt = score_tile(b, t)
                if not valid(j):
                    return
                n = 64 * j + 16 * g + 4 * qt + i
                dve.wait_ge(s_done, n + 1)
                nc.vector.reduce_max(maxes[:, g % 2, qt, i:i + 1], s_ps[:, i % 2, :], AX.X).then_inc(max_done, 1)
                if (qt, i) == (3, 3):
                    hi = max_split[:, g % 2, :, 0:4].bitcast(F32R)
                    dve.wait_ge(max_done, n + 1)
                    nc.vector.tensor_scalar(hi, maxes[:, g % 2, :, :], -1.0, None, ALU.mult).then_inc(max_hi_done, 1)
                    dve.wait_ge(max_hi_done, 4 * j + g + 1)
                    nc.vector.scalar_tensor_tensor(out=max_split[:, g % 2, :, 4:8].bitcast(F32R), in0=maxes[:, g % 2, :, :], scalar=-1.0,
                                                   in1=max_split[:, g % 2, :, 0:4], op0=ALU.mult, op1=ALU.subtract).then_inc(max_split_done, 1)

            def body(b):
                for t in range(QUARTERS):
                    for i in range(4):
                        maximum(b, t, i)
                        other(b, 4 * t + i)

            dve.wait_ge(x_in_loaded, 16)
            take_stats(LN_IN, x_in)
            aggregate(LN_IN, 0)
            normalise(LN_IN, 0, x_in, x_in)

            iterations(dve, body)

        @block.gpsimd
        def _(pool):
            pool_ops = nc.gpsimd
            pool_ops.memset(ident[:], 0.0).then_inc(consts_pool, 1)
            pool_ops.memset(ones_row, 1.0).then_inc(consts_pool, 1)
            pool_ops.memset(minus_half[:], -0.5).then_inc(consts_pool, 1)
            pool_ops.memset(v_cols[:, :, :, 1:2 * D:2], 1.0).then_inc(consts_pool, 1)
            pool.wait_ge(consts_pool, 1)
            pool_ops.affine_select(out=ident[:], in_=ident[:], compare_op=ALU.not_equal, fill=1.0, base=0,
                                   pattern=[[-1, P]], channel_multiplier=1).then_inc(consts_pool, 1)
            pool_ops.memset(k_rows[:, H // 2:H, :].bitcast(F32), 0.0).then_inc(consts_pool, 1)
            pool.wait_ge(small_loaded, 16 * 8)

            def inverse_deviation(ln, j):
                wait_apart(pool, (mean_done[ln], 4 * (j + 1)))
                pool_ops.tensor_scalar(rstd[ln][:], mean_var[ln][:, :, 1], EPS, None, ALU.add).then_inc(eps_added[ln], 1)
                pool.wait_ge(eps_added[ln], j + 1)
                pool_ops.tensor_tensor(rstd[ln][:], rstd[ln][:], minus_half[:], ALU.pow).then_inc(rstd_done[ln], 1)

            def split(j, dst, src, hi_done, split_done):
                pool.wait_ge(hi_done, j + 1)
                pool_ops.tensor_tensor(dst[:, 1, :], src, dst[:, 0, :].bitcast(F32), ALU.subtract).then_inc(split_done, 1)

            def split_hidden(dst, src, part):
                pool_ops.tensor_tensor(dst[:, 1, part, :], src[:, part, :], dst[:, 0, part, :].bitcast(F32), ALU.subtract).then_inc(hid_lo_pool, 1)

            def place_v(j, g):
                if not valid(j):
                    return
                pool.wait_ge(emptied["dve"], fill_count(j - 1, "v", "dve"))
                wait(pool, pv_done, 16 * (j - 1) + 4 * g + 4)
                for kt in range(NT):
                    src = v_tok[:, kt, 32 * g:32 * g + 32].rearrange("p (h d) -> p h d", d=D)
                    bias = v_bias[:, 32 * g:32 * g + 32].rearrange("p (h d) -> p h d", d=D)
                    last = pool_ops.tensor_tensor(v_cols[:, kt, 4 * g:4 * g + 4, 0:2 * D:2], src, bias, ALU.add)
                last.then_inc(v_placed, 1)

            def body(b):
                place_v(b, 3)
                if valid(b + 1):
                    split(b + 1, xT, turned[:], x_hi_done, xT_split)
                if valid(b - 3):
                    inverse_deviation(LN_OUT, b - 3)
                if valid(b - 1):
                    split(b - 1, oT, o_chan[:, 0, :], o_hi_done, oT_split)
                if valid(b - 3):
                    pool.wait_ge(normed[LN_OUT], 4 * (b - 2))
                    pool_ops.tensor_tensor(y_out[:], y_out[:], x_kept[:], ALU.add).then_inc(out_added, 1)
                if valid(b + 1):
                    pool.wait_ge(q_hi_done, b + 2)
                    pool_ops.tensor_tensor(q_split[:, 2, :], turned[:], q_split[:, 0, :].bitcast(F32), ALU.subtract).then_inc(q_split_done, 1)
                if valid(b - 1):
                    inverse_deviation(LN_POST, b - 1)
                    pool.wait_ge(normed[LN_POST], 4 * b)
                    pool.wait_ge(x_res_loaded, 16 * b)
                    wait(pool, x_mid_kept, b - 1)
                    pool_ops.tensor_tensor(x_mid[:], y_post[:], x_res[:], ALU.add).then_inc(x_mid_done, 1)
                if valid(b + 1):
                    pool.wait_ge(k_hi_done, b + 2)
                    pool_ops.tensor_tensor(k_split[:, 1, :], turned[:], k_split[:, 0, :].bitcast(F32), ALU.subtract).then_inc(k_split_done, 1)
                if valid(b - 1):
                    inverse_deviation(LN_MID, b - 1)
                place_v(b + 1, 0)
                if valid(b - 2):
                    for half in (0, 1):
                        pool.wait_ge(last_hi_done, 4 * (b - 2) + 2 * half + 2)
                        split_hidden(hid_b, acts, slice(2 * half, 2 * half + 2))
                if valid(b - 1):
                    split(b - 1, x2T, turned[:], x2_hi_done, x2T_split)
                    for o in range(HC):
                        pool.wait_ge(hid_hi_done, 6 * (b - 1) + o + 1)
                        split_hidden(hid_a, gated, slice(o, o + 1))
                place_v(b + 1, 1)
                if valid(b + 2):
                    inverse_deviation(LN_IN, b + 2)
                place_v(b + 1, 2)
                if valid(b - 1):
                    pool.wait_ge(hid_hi_done, 6 * (b - 1) + 6)
                    split_hidden(hid_a, acts, slice(2, 4))

            inverse_deviation(LN_IN, 0)
            iterations(pool, body)


INPUTS = ["L0_attn_x", "L0_attn_qkv_w", "L0_attn_qkv_b", "L0_attn_proj_w", "L0_attn_proj_b", "L0_ffn_w1_w", "L0_ffn_w1_s",
          "L0_ffn_w2_w", "L0_ffn_w2_s", "L0_ffn_h1_w", "L0_ffn_h1_s", "L0_ffn_h2_w", "L0_ffn_h2_s", "L0_ffn_w3_w", "L0_ffn_w3_s"]


def kernel(**inputs):
    import numpy as np
    import concourse.bacc as bacc
    from concourse.bass_utils import run_bass_kernel_spmd

    nc = bacc.Bacc("TRN2", target_bir_lowering=False, num_devices=1)
    arrays, args = {}, []
    for name in INPUTS:
        a = np.ascontiguousarray(inputs[name])
        arrays[f"in_{name}"] = a
        args.append(nc.dram_tensor(f"in_{name}", a.shape, mybir.dt.from_np(a.dtype), kind="ExternalInput").ap())
    args.append(nc.dram_tensor("out_x", (B, N, C), F32, kind="ExternalOutput").ap())
    build(nc, *args)
    r = run_bass_kernel_spmd(nc, [arrays], core_ids=[0])
    return r.results[0]["out_x"]
```

```python
import concourse.bass as bass
from concourse import mybir
from contextlib import ExitStack


F32 = mybir.dt.float32
F32R = mybir.dt.float32r
ALU = mybir.AluOpType
ACT = mybir.ActivationFunctionType
AX = mybir.AxisListType

B, N, C, H = 16, 512, 128, 16
D = C // H
P = 128
NT = N // P
G = H // 4
HID = 512
HC = HID // P
QROWS = 3 * 4 * D
MROWS = 8
QUARTERS = 4 * G
LEAD = 6
SCALE = float(D) ** -0.5
EPS = 1e-5
LN_IN, LN_POST, LN_MID, LN_OUT = range(4)

FILLS = (
    [("w3", -3, "act", 1), ("w3T", -3, "dve", 1), ("h2_0", -2, "act", 0), ("xT", 1, "act", 1), ("max1", 0, "act", 1),
     ("h2_1", -2, "act", 0), ("q", 1, "act", 1), ("proj", -1, "act", 1), ("projT", -1, "dve", 1), ("h2_2", -2, "act", 0),
     ("k", 1, "act", 1), ("max2", 0, "act", 1), ("h2_3", -2, "act", 0), ("v", 1, "dve", 1), ("x2T", -1, "act", 0)]
    + [(f"{n}{o}", -1, e, bank) for o in range(HC) for n, e, bank in (("gate", "act", 1), ("up", "dve", 0))]
    + [("max3", 0, "act", 1), ("h1_0", -1, "act", 0), ("h1_1", -1, "act", 0), ("max0", 1, "act", 1),
       ("h1_2", -1, "act", 0), ("h1_3", -1, "act", 0)]
)
H2_STEPS = [(0, 4, 4), (1, 8, 4), (2, 12, 8), (3, 20, 10)]
H1_STEPS = [(0, 44, 4), (1, 48, 4), (2, 52, 8), (3, 60, 4)]
MAX_TURNED = {11: 1, 27: 2, 43: 3, 59: 4}
ORDER = [f[0] for f in FILLS]
STEADY = 4


def sT_bank(u):
    return u % 3 if u < 53 else 0 if u == 53 else (u - 1) % 3


def valid(j):
    return not isinstance(j, int) or 0 <= j < B


def fills_before(b, engine=None):
    if isinstance(b, int):
        return sum(valid(c + off) for c in range(-1, b) for _, off, e, _ in FILLS if engine in (None, e))
    each = sum(engine in (None, e) for _, _, e, _ in FILLS)
    return b * each + (fills_before(STEADY, engine) - STEADY * each)


def fill_count(b, name, engine=None):
    upto = FILLS[:ORDER.index(name) + 1]
    return fills_before(b, engine) + sum(valid(b + off) for _, off, e, _ in upto if engine in (None, e))


def bank_of(name):
    return FILLS[ORDER.index(name)][3]


def fill_engine(name):
    return FILLS[ORDER.index(name)][2]


def bank_user_before(b, name):
    at = ORDER.index(name)
    for n, off, _, _ in reversed(FILLS[:at]):
        if bank_of(n) == bank_of(name) and valid(b + off):
            return b, n
    if isinstance(b, int) and b <= -1:
        return None
    for n, off, _, _ in reversed(FILLS):
        if bank_of(n) == bank_of(name) and valid(b - 1 + off):
            return b - 1, n
    return None


def wait(eng, sem, value):
    if not isinstance(value, int) or value > 0:
        eng.wait_ge(sem, value)


def build(nc, x, qkv_w, qkv_b, proj_w, proj_b, w1_w, w1_s, w2_w, w2_s, h1_w, h1_s, h2_w, h2_s, w3_w, w3_s, out):
    ctx = ExitStack()
    with ctx:
        def sb(name, shape, dt=F32):
            return ctx.enter_context(nc.sbuf_tensor(name, shape, dt))

        def sem(name):
            return ctx.enter_context(nc.semaphore(name))

        ident = sb("ident", [P, P])
        k_rows = sb("k_rows", [P, H, N], F32R)
        q_rows = sb("q_rows", [P, G, N], F32R)
        probs = sb("probs", [P, 2, 4, N])
        ones_row = probs[0:1, 0, :, :]
        v_cols = sb("v_cols", [P, NT, H, 2 * D])
        hid_a = sb("hid_a", [P, 2, HC, N], F32R)
        hid_b = sb("hid_b", [P, 2, HC, N], F32R)
        pre = sb("pre", [P, HC, N])
        gated = sb("gated", [P, HC, N])
        acts = sb("acts", [P, HC, N])
        w1T = sb("w1T", [P, 2, 1, HID], F32R)
        w2T = sb("w2T", [P, 2, 1, HID], F32R)
        h1T = sb("h1T", [P, 2, HC, HID], F32R)
        h2T = sb("h2T", [P, 2, HC, HID], F32R)
        w3T = sb("w3T", [P, 2, 1, HID], F32R)
        qkvp = sb("qkvp", [P, 2, 4 * C], F32R)
        qk_bias = sb("qk_bias", [P, 2])
        v_bias = sb("v_bias", [P, C])
        proj_bias = sb("proj_bias", [P, 1])
        s1 = sb("s1", [P, HC])
        s2 = sb("s2", [P, HC])
        s2_half = sb("s2_half", [P, HC])
        sh1 = sb("sh1", [P, HC])
        sh2 = sb("sh2", [P, HC])
        s3 = sb("s3", [P, 1])
        x_in = sb("x_in", [P, NT, C])
        x_res = sb("x_res", [P, NT, C])
        x_mid = sb("x_mid", [P, NT, C])
        x_kept = sb("x_kept", [P, NT, C])
        y_out = sb("y_out", [P, NT, C])
        turned = sb("turned", [P, N])
        xT = sb("xT", [P, 2, N], F32R)
        x2T = xT
        q_split = sb("q_split", [P, 3, N], F32R)
        k_split = sb("k_split", [P, 3, N], F32R)
        v_tok = sb("v_tok", [P, NT, C])
        maxes = sb("maxes", [P, 2, NT, 4])
        max_split = sb("max_split", [P, 2, NT, MROWS])
        o_group = sb("o_group", [P, N])
        o_chan = sb("o_chan", [P, 2, N])
        oT = sb("oT", [P, 2, N], F32R)
        y_post = o_chan[:, 0, :].rearrange("p (k c) -> p k c", c=C)
        mid_norm = y_post
        proj_out = o_chan[:, 1, :]
        ffn_out = turned
        stats = [sb(f"stats{n}", [P, NT, 6]) for n in range(4)]
        mean_var = [sb(f"mean_var{n}", [P, NT, 2]) for n in range(4)]
        rstd = [sb(f"rstd{n}", [P, NT]) for n in range(4)]
        minus_half = sb("minus_half", [P, NT])

        sT_ps = ctx.enter_context(nc.psum_tensor("sT_ps", [P, 3, N], F32))
        s_ps = ctx.enter_context(nc.psum_tensor("s_ps", [P, 2, N], F32))
        o_ps = ctx.enter_context(nc.psum_tensor("o_ps", [P, N], F32))
        fill_ps = ctx.enter_context(nc.psum_tensor("fill_ps", [P, 2, N], F32))

        qkvp_loaded = sem("qkvp_loaded")
        rows_loaded = sem("rows_loaded")
        small_loaded = sem("small_loaded")
        ones_placed = sem("ones_placed")
        consts_pool = sem("consts_pool")
        zeros_dve = sem("zeros_dve")
        wT_turned = sem("wT_turned")
        halved = sem("halved")
        w_hi = sem("w_hi")
        w_lo = sem("w_lo")
        x_in_loaded = sem("x_in_loaded")
        x_res_loaded = sem("x_res_loaded")
        kq_moved = [sem(f"kq_moved{g}") for g in range(G)]
        o_moved = sem("o_moved")
        out_stored = sem("out_stored")
        sT_done = sem("sT_done")
        s_done = sem("s_done")
        pv_done = sem("pv_done")
        fill_done = sem("fill_done")
        exp_done = sem("exp_done")
        emptied = {"act": sem("emptied_act"), "dve": sem("emptied_dve")}
        tanh_done = sem("tanh_done")
        gelu_done = sem("gelu_done")
        max_done = sem("max_done")
        max_hi_done = sem("max_hi_done")
        max_split_done = sem("max_split_done")
        o_emptied = sem("o_emptied")
        stats_done = [sem(f"stats_done{n}") for n in range(4)]
        mean_done = [sem(f"mean_done{n}") for n in range(4)]
        eps_added = [sem(f"eps_added{n}") for n in range(4)]
        rstd_done = [sem(f"rstd_done{n}") for n in range(4)]
        normed = [sem(f"normed{n}") for n in range(4)]
        sums_inverted = sem("sums_inverted")
        o_scaled = sem("o_scaled")
        o_hi_done = sem("o_hi_done")
        oT_split = sem("oT_split")
        x_hi_done = sem("x_hi_done")
        xT_split = sem("xT_split")
        x2_hi_done = sem("x2_hi_done")
        x2T_split = sem("x2T_split")
        q_hi_done = sem("q_hi_done")
        q_split_done = sem("q_split_done")
        k_hi_done = sem("k_hi_done")
        k_split_done = sem("k_split_done")
        v_placed = sem("v_placed")
        x_mid_done = sem("x_mid_done")
        x_mid_kept = sem("x_mid_kept")
        out_added = sem("out_added")
        silu_done = sem("silu_done")
        hid_hi_done = sem("hid_hi_done")
        last_hi_done = sem("last_hi_done")
        last_lo_done = sem("last_lo_done")
        hid_lo_dve = sem("hid_lo_dve")
        hid_lo_pool = sem("hid_lo_pool")

        xr = x.rearrange("b (k p) c -> b p k c", p=P)
        outr = out.rearrange("b (k p) c -> b p k c", p=P)

        def turned_weights():
            yield [pre[:, 0, P * o:P * o + P] for o in range(HC)], w1T, 0
            yield [pre[:, 1, P * o:P * o + P] for o in range(HC)], w2T, 0
            yield [pre[:, 2, P * k:P * k + P] for k in range(HC)], w3T, 0
            for src, dst in ((gated, h1T), (acts, h2T)):
                for k in range(HC):
                    yield [src[:, o, P * k:P * k + P] for o in range(HC)], dst, k

        TURNED = 3 + 2 * HC
        WEIGHT_STEP = 46
        block = ctx.enter_context(nc.Block())

        counted = {eng.engine: [eng.alloc_register(f"counted{n}") for n in range(1 + G)]
                   for eng in (nc.sync, nc.vector, nc.gpsimd)}

        def wait_apart(eng, *counts):
            ready = []
            for n, (q, v) in enumerate(counts):
                if not isinstance(v, int):
                    eng.reg_mov(counted[eng.engine][n], v)
                    v = counted[eng.engine][n]
                ready.append((q, v))
            eng.wait_ge(consts_pool, 6)
            for q, v in ready:
                wait(eng, q, v)

        def iterations(eng, body):
            for b in range(-1, STEADY):
                body(b)
            with eng.Fori(STEADY, B - 2) as b:
                body(b)
            for b in range(B - 2, B + 3):
                body(b)

        def score_tile(b, t):
            s = t + LEAD
            j = b + s // QUARTERS
            return j, s % QUARTERS // 4, s % 4

        @block.sync
        def _(sp):
            sp.dma_start(x_in[:], xr[0]).then_inc(x_in_loaded, 16)
            sp.dma_start(pre[:, 3, :384], qkv_w).then_inc(qkvp_loaded, 16)
            sp.dma_start(pre[:, 3, 384:], proj_w).then_inc(qkvp_loaded, 16)
            sp.dma_start(pre[:, 0, :].rearrange("p (o i) -> p o i", i=C), w1_w.rearrange("(o p) i -> p o i", p=P)).then_inc(rows_loaded, 16)
            sp.dma_start(pre[:, 1, :].rearrange("p (o i) -> p o i", i=C), w2_w.rearrange("(o p) i -> p o i", p=P)).then_inc(rows_loaded, 16)
            sp.dma_start(pre[:, 2, :], w3_w).then_inc(rows_loaded, 16)
            sp.dma_start(gated[:], h1_w.rearrange("(o p) i -> p o i", p=P)).then_inc(rows_loaded, 16)
            sp.dma_start(acts[:], h2_w.rearrange("(o p) i -> p o i", p=P)).then_inc(rows_loaded, 16)
            sp.dma_start(qk_bias[:], qkv_b[0:2 * C].rearrange("(a p) -> p a", p=P), allow_slow_non_contiguous=True).then_inc(small_loaded, 16)
            sp.dma_start(v_bias[:], qkv_b[2 * C:3 * C].rearrange("(a c) -> a c", a=1).broadcast_to([P, C])).then_inc(small_loaded, 16)
            sp.dma_start(proj_bias[:], proj_b.rearrange("(a p) -> p a", p=P), allow_slow_non_contiguous=True).then_inc(small_loaded, 16)
            for dst, src in ((s1, w1_s), (s2, w2_s), (sh1, h1_s), (sh2, h2_s), (s3, w3_s)):
                sp.dma_start(dst[:], src.rearrange("(a p) -> p a", p=P), allow_slow_non_contiguous=True).then_inc(small_loaded, 16)
            sp.wait_ge(consts_pool, 6)
            sp.wait_ge(zeros_dve, 1)
            for i in range(4):
                for row in (QROWS + i, QROWS + 4 + i):
                    sp.dma_start(k_rows[row:row + 1].rearrange("p (g i) n -> p g i n", i=4)[:, :, i, :].bitcast(F32),
                                 ones_row).then_inc(ones_placed, 16)

            def move_kq(j, g):
                if not valid(j):
                    return
                wait_apart(sp, (k_split_done, j + 1), (sT_done, (j - 1) * 64 + 16 * g + 16))
                sp.dma_start(q_rows[0:QROWS, g, :].bitcast(F32), q_split[32 * g:32 * g + 32].bitcast(F32)).then_inc(kq_moved[g], 16)
                for i in range(4):
                    h = 4 * g + i
                    sp.dma_start(k_rows[24 * i:24 * i + 24, h, :].bitcast(F32), k_split[D * h:D * h + D].bitcast(F32)).then_inc(kq_moved[g], 16)

            def move_o(j, g):
                if not valid(j):
                    return
                wait_apart(sp, (o_emptied, 4 * j + g + 1), (o_scaled, j),
                           *([(emptied["act"], fill_count(j, "x2T", "act"))] if valid(j - 1) else []))
                for i in range(4):
                    h = 4 * g + i
                    sp.dma_start(o_chan[D * h:D * h + D], o_group[32 * i:32 * i + 2 * D, :]).then_inc(o_moved, 16)

            def body(b):
                move_kq(b, 3)
                move_o(b - 1, 3)
                if valid(b + 2) and (not isinstance(b, int) or b + 2 >= 1):
                    wait_apart(sp, (emptied["act"], fill_count(b, "xT", "act")))
                    sp.dma_start(x_in[:], xr[b + 2]).then_inc(x_in_loaded, 16)
                if valid(b):
                    wait_apart(sp, (x_mid_done, b))
                    sp.dma_start(x_res[:], xr[b]).then_inc(x_res_loaded, 16)
                if valid(b - 3):
                    wait_apart(sp, (out_added, b - 2))
                    sp.dma_start(outr[b - 3], y_out[:]).then_inc(out_stored, 16)
                move_kq(b + 1, 0)
                move_o(b, 0)
                for g in (1, 2):
                    move_kq(b + 1, g)
                    move_o(b, g)

            iterations(sp, body)
            sp.wait_ge(out_stored, 16 * B)

        @block.tensor
        def _(pe):
            pe.wait_ge(consts_pool, 5)
            pe.wait_ge(w_lo, 1)
            pe.wait_ge(ones_placed, 16 * 8)
            pe.wait_ge(zeros_dve, 2)

            def turn_weights(n, blocks):
                if n == 0:
                    pe.wait_ge(rows_loaded, 16 * 5)
                    for task in ("max3", "k"):
                        wait(pe, emptied["act"], fill_count(0, task, "act"))
                if n >= 2:
                    pe.wait_ge(w_lo, n)
                for c, src in enumerate(blocks):
                    last = nc.tensor.transpose(fill_ps[:, n % 2, P * c:P * c + P], src, ident[:])
                last.then_inc(wT_turned, 1)

            def begin(b, name):
                before = bank_user_before(b, name)
                if before:
                    e = fill_engine(before[1])
                    wait(pe, emptied[e], fill_count(*before, e))
                return fill_ps[:, bank_of(name), :]

            def split_product(bank, pairs, part=(0, 1)):
                terms = [(w, xs, u, v) for w, xs in pairs for u, v in ((0, 0), (1, 0), (0, 1))]
                n = len(terms)
                for a in range(part[0] * n // part[1], (part[0] + 1) * n // part[1]):
                    w, xs, u, v = terms[a]
                    last = nc.tensor.matmul(bank, w(u), xs(v), start=(a == 0), stop=(a == n - 1))
                return last

            def hidden(b, layer, w, src, plan, u):
                o, start, steps = next(c for c in plan if c[1] <= u < c[1] + c[2])
                name = f"{layer}_{o}"
                bank = begin(b, name) if u == start else fill_ps[:, bank_of(name), :]
                last = split_product(bank, [(lambda u, k=k: w[:, u, k, P * o:P * o + P], lambda v, k=k: src[:, v, k, :])
                                            for k in range(HC)], (u - start, steps))
                if u == start + steps - 1:
                    last.then_inc(fill_done, 1)

            def turn(b, name, src):
                bank = begin(b, name)
                for k in range(NT):
                    last = nc.tensor.transpose(bank[:, P * k:P * k + P], src(k), ident[:])
                last.then_inc(fill_done, 1)

            def fill(b, u):
                if isinstance(b, int) and b == 0 and WEIGHT_STEP <= u < WEIGHT_STEP + TURNED:
                    turn_weights(u - WEIGHT_STEP, list(turned_weights())[u - WEIGHT_STEP][0])
                if isinstance(b, int) and b == 0 and u == 59:
                    pe.wait_ge(w_lo, TURNED + 1)
                if u == 6 and valid(b - 3):
                    wait(pe, emptied["act"], fill_count(b, "w3", "act"))
                    turn(b, "w3T", lambda k: ffn_out[:, P * k:P * k + P])
                if u == 8 and valid(b + 1):
                    wait(pe, normed[LN_IN], 4 * (b + 2))
                    turn(b, "xT", lambda k: x_in[:, k, :])
                if u in (12, 24) and valid(b + 1):
                    wait(pe, xT_split, b + 2)
                    a = u // 24
                    split_product(begin(b, "qk"[a]), [(lambda u: qkvp[:, u, C * a:C * a + C], lambda v: xT[:, v, :])]).then_inc(fill_done, 1)
                if u in MAX_TURNED:
                    g = MAX_TURNED[u]
                    if valid(b + g // 4):
                        wait(pe, max_split_done, 4 * b + g + 1)
                        bank = begin(b, f"max{g % 4}")
                        for k in range(NT):
                            last = nc.tensor.transpose(bank[0:MROWS, P * k:P * k + P], max_split[:, g % 2, k, :], ident[:])
                        last.then_inc(fill_done, 1)
                if u == 16 and valid(b - 1):
                    wait(pe, oT_split, b)
                    split_product(begin(b, "proj"), [(lambda u: qkvp[:, u, 3 * C:4 * C], lambda v: oT[:, v, :])]).then_inc(fill_done, 1)
                if u == 18 and valid(b - 1):
                    wait(pe, emptied["act"], fill_count(b, "proj", "act"))
                    turn(b, "projT", lambda k: proj_out[:, P * k:P * k + P])
                if 4 <= u < 30 and valid(b - 2):
                    if u < 8:
                        wait(pe, *((hid_lo_dve, 3 * (b - 2) + u - 2) if u < 6 else (hid_lo_pool, 5 * (b - 2) + u - 2)))
                    hidden(b, "h2", h2T, hid_a, H2_STEPS, u)
                if 28 <= u < 32 and valid(b + 1):
                    k = u - 28
                    bank = begin(b, "v") if k == 0 else fill_ps[:, bank_of("v"), :]
                    last = split_product(bank[:, P * k:P * k + P],
                                         [(lambda u: xT[:, u, P * k:P * k + P], lambda v: qkvp[:, v, 2 * C:3 * C])])
                    if k == NT - 1:
                        last.then_inc(fill_done, 1)
                if u == 32 and valid(b - 1):
                    wait(pe, normed[LN_MID], 4 * b)
                    turn(b, "x2T", lambda k: mid_norm[:, k, :])
                if 35 <= u < 43 and valid(b - 1):
                    o = (u - 35) // 2
                    wait(pe, x2T_split, b)
                    name, w = (("up", w2T), ("gate", w1T))[u % 2]
                    split_product(begin(b, f"{name}{o}"), [(lambda u: w[:, u, 0, P * o:P * o + P], lambda v: x2T[:, v, :])]).then_inc(fill_done, 1)
                if u >= 44 and valid(b - 1):
                    if u < 47:
                        wait(pe, hid_lo_pool, 5 * (b - 1) + u - 43)
                    if u == 47:
                        wait(pe, hid_lo_dve, 3 * (b - 1) + 1)
                    hidden(b, "h1", h1T, hid_a, H1_STEPS, u)
                if u < 4 and valid(b - 3):
                    if u == 0:
                        wait(pe, last_lo_done, 2 * (b - 2))
                        begin(b, "w3")
                    last = split_product(fill_ps[:, bank_of("w3"), :], [(lambda u, k=k: w3T[:, u, 0, P * k:P * k + P],
                                                                         lambda v, k=k: hid_b[:, v, k, :]) for k in range(HC)],
                                         (u, 4))
                    if u == 3:
                        last.then_inc(fill_done, 1)

            def transposed_scores(b, t, i):
                g, kt, h, n = t // 4, t % 4, t // 4 * 4 + i, 64 * b + 4 * t + i
                if kt == 0 and i == 0:
                    at = (b - 1, "max0") if g == 0 else (b, f"max{g}")
                    wait(pe, emptied["act"], fill_count(*at, "act"))
                u = 4 * t + i
                wait(pe, exp_done, n + 1 - {53: 2, 54: 4, 55: 2, 56: 4}.get(u, 3))
                nc.tensor.matmul(sT_ps[:, sT_bank(u), :], k_rows[0:QROWS + MROWS, h, P * kt:P * kt + P],
                                 q_rows[0:QROWS + MROWS, g, :], start=True, stop=True).then_inc(sT_done, 1)

            def scores(b, t, i):
                j, g, qt = score_tile(b, t)
                if not valid(j):
                    return
                if qt == 0 and i == 0:
                    wait(pe, kq_moved[g], 80 * (j + 1))
                wait(pe, max_done, 64 * j + 16 * g + 4 * qt + i - 1)
                nc.tensor.matmul(s_ps[:, i % 2, :], q_rows[0:QROWS, g, P * qt:P * qt + P],
                                 k_rows[0:QROWS, 4 * g + i, :], start=True, stop=True).then_inc(s_done, 1)

            def outputs(j, t):
                if not valid(j):
                    return
                g, kt = t // 4, t % 4
                if kt == 0:
                    wait(pe, o_emptied, 4 * j + g)
                    wait(pe, v_placed, 4 * j + g + 1)
                wait(pe, exp_done, 64 * j + 4 * t + 4)
                for i in range(4):
                    last = nc.tensor.matmul(o_ps[32 * i:32 * i + 2 * D, :], v_cols[:, kt, 4 * g + i, :], probs[:, t % 2, i, :],
                                            start=(kt == 0), stop=(kt == 3))
                last.then_inc(pv_done, 1)

            def body(b):
                for t in range(QUARTERS):
                    for i in range(4):
                        if valid(b):
                            transposed_scores(b, t, i)
                        scores(b, t, i)
                        fill(b, 4 * t + i)
                    outputs(b - 1 if t == 0 else b, (t - 1) % QUARTERS)

            iterations(pe, body)

        @block.scalar
        def _(act):
            act.wait_ge(small_loaded, 16 * 8)

            def empty(b, name, dst, src=None, rows=P, **kw):
                act.wait_ge(fill_done, fill_count(b, name))
                src = fill_ps[0:rows, bank_of(name), :]
                nc.scalar.activation(dst, src, ACT.Identity, **kw).then_inc(emptied["act"], 1)

            def gelu(last):
                act.wait_ge(emptied["act"], last)
                for half in (slice(0, 2), slice(2, 4)):
                    nc.scalar.activation(acts[:, half, :], pre[:, half, :], ACT.Gelu).then_inc(gelu_done, 1)

            def empty_h2(b, o):
                empty(b, f"h2_{o}", pre[:, o, :], scale=sh2[:, o:o + 1])

            def empty_maxima(b, g):
                empty(b, f"max{g}", q_rows[QROWS:QROWS + MROWS, g, :], rows=MROWS)

            def other(b, u):
                if u == 0 and valid(b - 2):
                    if valid(b - 3):
                        wait(act, last_lo_done, 2 * (b - 2))
                    gelu(fill_count(b - 1, "h1_3", "act"))
                if u == 3 and valid(b - 3):
                    wait(act, x2T_split, min(b - 1, B) if isinstance(b, int) else b - 1)
                    empty(b, "w3", ffn_out[:], scale=s3[:, 0:1])
                if u == 7 and valid(b - 2):
                    empty_h2(b, 0)
                if u == 8 and valid(b + 1):
                    wait(act, x2T_split, b - 1)
                    empty(b, "xT", turned[:])
                if u == 12 and valid(b + 1):
                    wait(act, xT_split, b + 2)
                    empty(b, "q", turned[:], bias=qk_bias[:, 0:1])
                if u in MAX_TURNED:
                    g = MAX_TURNED[u]
                    if valid(b + g // 4):
                        empty_maxima(b, g % 4)
                if u == 16 and valid(b - 1):
                    empty(b, "proj", proj_out[:], bias=proj_bias[:, 0:1])
                if u in (11, 19, 29) and valid(b - 2):
                    empty_h2(b, {11: 1, 19: 2, 29: 3}[u])
                if u == 20 and valid(b - 2):
                    wait(act, x_mid_done, b - 1)
                    wait(act, out_added, b - 2)
                    nc.scalar.activation(x_kept[:], x_mid[:], ACT.Identity).then_inc(x_mid_kept, 1)
                if u == 24 and valid(b + 1):
                    wait(act, q_split_done, b + 2)
                    empty(b, "k", turned[:], bias=qk_bias[:, 1:2])
                if u == 32 and valid(b - 1):
                    wait(act, k_split_done, min(b + 2, B) if isinstance(b, int) else b + 2)
                    empty(b, "x2T", turned[:])
                if u == 32 and valid(b - 2):
                    gelu(fill_count(b, "h2_3", "act"))
                if u in (35, 37, 39, 41) and valid(b - 1):
                    o = (u - 35) // 2
                    if u == 35 and valid(b - 2):
                        wait(act, gelu_done, 4 * (b - 1))
                    empty(b, f"gate{o}", pre[:, o, :], scale=s1[:, o:o + 1])
                if u in (37, 39, 41, 43) and valid(b - 1):
                    o = (u - 37) // 2
                    act.wait_ge(emptied["act"], fill_count(b, f"gate{o}", "act"))
                    act.wait_ge(emptied["dve"], fill_count(b, f"up{o}", "dve"))
                    nc.scalar.activation(pre[:, o, :], pre[:, o, :], ACT.Tanh, scale=0.5).then_inc(tanh_done, 1)
                if u in (44, 45, 46, 48) and valid(b - 2):
                    k = min(u - 44, 3)
                    if k % 2 == 0:
                        wait(act, gelu_done, 4 * (b - 2) + 3 + k // 2)
                    nc.scalar.activation(hid_b[:, 0, k, :], acts[:, k, :], ACT.Identity).then_inc(last_hi_done, 1)
                if u in (47, 51, 59, 63) and valid(b - 1):
                    o = (47, 51, 59, 63).index(u)
                    empty(b, f"h1_{o}", pre[:, o, :], scale=sh1[:, o:o + 1])

            def body(b):
                for t in range(QUARTERS):
                    for i in range(4):
                        u = 4 * t + i
                        if valid(b):
                            if i == 0:
                                wait(act, pv_done, 16 * b + t - 1)
                            act.wait_ge(sT_done, 64 * b + u + 1)
                            nc.scalar.activation(probs[:, t % 2, i, :], sT_ps[:, sT_bank(u), :], ACT.Exp,
                                                 scale=SCALE).then_inc(exp_done, 1)
                        other(b, u)

            iterations(act, body)

        @block.vector
        def _(dve):
            nc.vector.memset(k_rows[:, 0:H // 2, :].bitcast(F32), 0.0).then_inc(zeros_dve, 1)
            nc.vector.memset(o_ps[:], 0.0).then_inc(zeros_dve, 1)
            dve.wait_ge(qkvp_loaded, 16 * 2)
            nc.vector.tensor_copy(qkvp[:, 0, :], pre[:, 3, :]).then_inc(w_hi, 1)
            dve.wait_ge(w_hi, 1)
            nc.vector.tensor_tensor(qkvp[:, 1, :], pre[:, 3, :], qkvp[:, 0, :].bitcast(F32), ALU.subtract).then_inc(w_lo, 1)

            def split_weights(n, dst, k):
                dve.wait_ge(wT_turned, n + 1)
                nc.vector.tensor_copy(dst[:, 0, k, :], fill_ps[:, n % 2, :]).then_inc(w_hi, 1)
                dve.wait_ge(w_hi, n + 2)
                nc.vector.tensor_tensor(dst[:, 1, k, :], fill_ps[:, n % 2, :], dst[:, 0, k, :].bitcast(F32), ALU.subtract).then_inc(w_lo, 1)

            def take_stats(ln, src, tiles=range(NT)):
                for k in tiles:
                    nc.vector.bn_stats(stats[ln][:, k, :], src[:, k, :]).then_inc(stats_done[ln], 1)

            def aggregate(ln, j):
                wait_apart(dve, (stats_done[ln], 4 * (j + 1)))
                for k in range(NT):
                    nc.vector.bn_aggr(mean_var[ln][:, k, :], stats[ln][:, k, :]).then_inc(mean_done[ln], 1)

            def normalise(ln, j, dst, src, tiles=range(NT)):
                dve.wait_ge(rstd_done[ln], j + 1)
                for k in tiles:
                    nc.vector.tensor_scalar(dst[:, k, :], src[:, k, :], mean_var[ln][:, k, 0:1], rstd[ln][:, k:k + 1],
                                            ALU.subtract, ALU.mult).then_inc(normed[ln], 1)

            def tokens(a):
                return a[:].rearrange("p (k c) -> p k c", c=C)

            def twice(a):
                return a[:].rearrange("p (a n) -> p a n", a=1).broadcast_to([P, 2, N])

            def empty_o(j, g):
                if not valid(j):
                    return
                dve.wait_ge(pv_done, 16 * j + 4 * g + 4)
                wait(dve, o_moved, 64 * (4 * j + g))
                nc.vector.tensor_copy(o_group[:], o_ps[:]).then_inc(o_emptied, 1)

            def split_hi(dst, src, part):
                nc.vector.tensor_copy(dst[:, 0, part, :], src[:, part, :]).then_inc(hid_hi_done, 1)

            def split_lo(dst, src, part):
                nc.vector.tensor_tensor(dst[:, 1, part, :], src[:, part, :], dst[:, 0, part, :].bitcast(F32), ALU.subtract).then_inc(hid_lo_dve, 1)

            def other(b, u):
                if isinstance(b, int) and b == 0 and WEIGHT_STEP <= u < WEIGHT_STEP + TURNED:
                    n = u - WEIGHT_STEP
                    split_weights(n, *list(turned_weights())[n][1:])
                if u == 2 and valid(b - 2):
                    wait_apart(dve, (gelu_done, 4 * (b - 2) + 1))
                    split_hi(hid_a, acts, slice(0, 2))
                if u == 3 and valid(b - 2):
                    dve.wait_ge(hid_hi_done, 6 * (b - 2) + 5)
                    split_lo(hid_a, acts, slice(0, 1))
                    wait_apart(dve, (gelu_done, 4 * (b - 2) + 2))
                    split_hi(hid_a, acts, slice(2, 4))
                    split_lo(hid_a, acts, slice(1, 2))
                if u == 7 and valid(b - 3):
                    dve.wait_ge(fill_done, fill_count(b, "w3T"))
                    wait(dve, out_stored, 16 * (b - 3))
                    nc.vector.tensor_copy(y_out[:], tokens_of_bank("w3T")).then_inc(emptied["dve"], 1)
                if u == 4:
                    empty_o(b - 1, 3)
                if u in (21, 37, 53):
                    empty_o(b, (u - 20) // 16)
                if u in (12, 13) and valid(b - 3):
                    dve.wait_ge(emptied["dve"], fill_count(b, "w3T", "dve"))
                    take_stats(LN_OUT, y_out, range(2 * u - 24, 2 * u - 22))
                if u == 9 and valid(b + 1):
                    wait_apart(dve, (emptied["act"], fill_count(b, "xT", "act")))
                    nc.vector.tensor_copy(xT[:, 0, :], turned[:]).then_inc(x_hi_done, 1)
                if u == 13 and valid(b - 3):
                    aggregate(LN_OUT, b - 3)
                if 8 <= u < 12 and valid(b - 1):
                    dve.wait_ge(o_moved, 256 * b)
                    part = slice(P * (u - 8), P * (u - 7))
                    nc.vector.reciprocal(o_chan[:, 1, part], o_chan[:, 1, part]).then_inc(sums_inverted, 1)
                if u == 12 and valid(b - 1):
                    dve.wait_ge(sums_inverted, 4 * b)
                    nc.vector.tensor_tensor(o_chan[:, 0, :], o_chan[:, 0, :], o_chan[:, 1, :], ALU.mult).then_inc(o_scaled, 1)
                    wait_apart(dve, (o_scaled, b), (oT_split, b - 1))
                    nc.vector.tensor_copy(oT[:, 0, :], o_chan[:, 0, :]).then_inc(o_hi_done, 1)
                if u == 15 and valid(b + 1):
                    wait_apart(dve, (emptied["act"], fill_count(b, "q", "act")),
                               *((kq_moved[g], 80 * (b + 1)) for g in range(G)))
                    nc.vector.tensor_copy(q_split[:, 0:2, :], twice(turned)).then_inc(q_hi_done, 1)
                if u in (16, 17) and valid(b - 3):
                    normalise(LN_OUT, b - 3, y_out, y_out, range(2 * u - 32, 2 * u - 30))
                if u == 19 and valid(b - 1):
                    dve.wait_ge(fill_done, fill_count(b, "projT"))
                    nc.vector.tensor_copy(y_post[:], tokens_of_bank("projT")).then_inc(emptied["dve"], 1)
                    dve.wait_ge(emptied["dve"], fill_count(b, "projT", "dve"))
                    take_stats(LN_POST, y_post, range(0, 2))
                if u == 20 and valid(b - 1):
                    take_stats(LN_POST, y_post, range(2, 4))
                    aggregate(LN_POST, b - 1)
                if u in (22, 23) and valid(b - 1):
                    normalise(LN_POST, b - 1, y_post, y_post, range(2 * u - 44, 2 * u - 42))
                if u in (26, 27) and valid(b - 1):
                    dve.wait_ge(x_mid_done, b)
                    take_stats(LN_MID, x_mid, range(2 * u - 52, 2 * u - 50))
                if u == 28:
                    if valid(b - 1):
                        aggregate(LN_MID, b - 1)
                if u == 33 and valid(b + 1):
                    dve.wait_ge(fill_done, fill_count(b, "v"))
                    wait(dve, v_placed, 4 * (b + 1))
                    nc.vector.tensor_copy(v_tok[:], tokens_of_bank("v")).then_inc(emptied["dve"], 1)
                if u == 25 and valid(b + 1):
                    wait_apart(dve, (emptied["act"], fill_count(b, "k", "act")))
                    nc.vector.tensor_copy(k_split[:, 0:3:2, :], twice(turned)).then_inc(k_hi_done, 1)
                if u in (30, 31) and valid(b - 1):
                    normalise(LN_MID, b - 1, mid_norm, x_mid, range(2 * u - 60, 2 * u - 58))
                if u == 33 and valid(b - 1):
                    wait_apart(dve, (emptied["act"], fill_count(b, "x2T", "act")))
                    nc.vector.tensor_copy(x2T[:, 0, :], turned[:]).then_inc(x2_hi_done, 1)
                if valid(b - 1) and 36 <= u <= 42 and u % 2 == 0:
                    o = (u - 36) // 2
                    dve.wait_ge(fill_done, fill_count(b, f"up{o}"))
                    dve.wait_ge(emptied["act"], fill_count(b, f"gate{o}", "act"))
                    nc.vector.scalar_tensor_tensor(out=gated[:, o, :], in0=fill_ps[:, bank_of(f"up{o}"), :], scalar=s2_half[:, o:o + 1],
                                                   in1=pre[:, o, :], op0=ALU.mult, op1=ALU.mult).then_inc(emptied["dve"], 1)
                if valid(b - 1) and 38 <= u <= 44 and u % 2 == 0:
                    o = (u - 38) // 2
                    wait(dve, tanh_done, 4 * (b - 1) + o + 1)
                    wait(dve, emptied["dve"], fill_count(b, f"up{o}", "dve"))
                    nc.vector.scalar_tensor_tensor(out=gated[:, o, :], in0=pre[:, o, :], scalar=1.0, in1=gated[:, o, :], op0=ALU.add,
                                                   op1=ALU.mult).then_inc(silu_done, 1)
                if valid(b - 1) and 39 <= u <= 45 and u % 2:
                    o = (u - 39) // 2
                    wait_apart(dve, (silu_done, 4 * (b - 1) + o + 1))
                    split_hi(hid_a, gated, slice(o, o + 1))
                    if o == HC - 1:
                        dve.wait_ge(hid_hi_done, 6 * (b - 1) + 4)
                        split_lo(hid_a, gated, slice(o, o + 1))
                if u in (48, 49) and valid(b + 2):
                    dve.wait_ge(x_in_loaded, 16 * (b + 3))
                    take_stats(LN_IN, x_in, range(2 * u - 96, 2 * u - 94))
                if u == 50 and valid(b + 2):
                    aggregate(LN_IN, b + 2)
                if u in (54, 56) and valid(b + 2):
                    normalise(LN_IN, b + 2, x_in, x_in, range(u - 54, u - 52))
            def tokens_of_bank(name):
                return fill_ps[:, bank_of(name), :].rearrange("p (k c) -> p k c", c=C)

            def maximum(b, t, i):
                j, g, qt = score_tile(b, t)
                if not valid(j):
                    return
                n = 64 * j + 16 * g + 4 * qt + i
                dve.wait_ge(s_done, n + 1)
                nc.vector.reduce_max(maxes[:, g % 2, qt, i:i + 1], s_ps[:, i % 2, :], AX.X).then_inc(max_done, 1)
                if (qt, i) == (3, 3):
                    hi = max_split[:, g % 2, :, 0:4].bitcast(F32R)
                    dve.wait_ge(max_done, n + 1)
                    nc.vector.tensor_scalar(hi, maxes[:, g % 2, :, :], -1.0, None, ALU.mult).then_inc(max_hi_done, 1)
                    dve.wait_ge(max_hi_done, 4 * j + g + 1)
                    nc.vector.scalar_tensor_tensor(out=max_split[:, g % 2, :, 4:8].bitcast(F32R), in0=maxes[:, g % 2, :, :], scalar=-1.0,
                                                   in1=max_split[:, g % 2, :, 0:4], op0=ALU.mult, op1=ALU.subtract).then_inc(max_split_done, 1)

            def body(b):
                for t in range(QUARTERS):
                    for i in range(4):
                        maximum(b, t, i)
                        other(b, 4 * t + i)

            dve.wait_ge(small_loaded, 16 * 8)
            nc.vector.tensor_scalar(s2_half[:], s2[:], 0.5, None, ALU.mult).then_inc(halved, 1)
            dve.wait_ge(halved, 1)
            dve.wait_ge(x_in_loaded, 16)
            take_stats(LN_IN, x_in)
            aggregate(LN_IN, 0)
            normalise(LN_IN, 0, x_in, x_in)

            iterations(dve, body)

        @block.gpsimd
        def _(pool):
            pool_ops = nc.gpsimd
            pool_ops.memset(ident[:], 0.0).then_inc(consts_pool, 1)
            pool_ops.memset(ones_row, 1.0).then_inc(consts_pool, 1)
            pool_ops.memset(minus_half[:], -0.5).then_inc(consts_pool, 1)
            pool_ops.memset(v_cols[:, :, :, 1:2 * D:2], 1.0).then_inc(consts_pool, 1)
            pool.wait_ge(consts_pool, 1)
            pool_ops.affine_select(out=ident[:], in_=ident[:], compare_op=ALU.not_equal, fill=1.0, base=0,
                                   pattern=[[-1, P]], channel_multiplier=1).then_inc(consts_pool, 1)
            pool_ops.memset(k_rows[:, H // 2:H, :].bitcast(F32), 0.0).then_inc(consts_pool, 1)
            pool.wait_ge(small_loaded, 16 * 8)

            def inverse_deviation(ln, j):
                wait_apart(pool, (mean_done[ln], 4 * (j + 1)))
                pool_ops.tensor_scalar(rstd[ln][:], mean_var[ln][:, :, 1], EPS, None, ALU.add).then_inc(eps_added[ln], 1)
                pool.wait_ge(eps_added[ln], j + 1)
                pool_ops.tensor_tensor(rstd[ln][:], rstd[ln][:], minus_half[:], ALU.pow).then_inc(rstd_done[ln], 1)

            def split(j, dst, src, hi_done, split_done):
                pool.wait_ge(hi_done, j + 1)
                pool_ops.tensor_tensor(dst[:, 1, :], src, dst[:, 0, :].bitcast(F32), ALU.subtract).then_inc(split_done, 1)

            def split_hidden(dst, src, part):
                return pool_ops.tensor_tensor(dst[:, 1, part, :], src[:, part, :], dst[:, 0, part, :].bitcast(F32), ALU.subtract)

            def place_v(j, g):
                if not valid(j):
                    return
                pool.wait_ge(emptied["dve"], fill_count(j - 1, "v", "dve"))
                wait(pool, pv_done, 16 * (j - 1) + 4 * g + 4)
                for kt in range(NT):
                    src = v_tok[:, kt, 32 * g:32 * g + 32].rearrange("p (h d) -> p h d", d=D)
                    bias = v_bias[:, 32 * g:32 * g + 32].rearrange("p (h d) -> p h d", d=D)
                    last = pool_ops.tensor_tensor(v_cols[:, kt, 4 * g:4 * g + 4, 0:2 * D:2], src, bias, ALU.add)
                last.then_inc(v_placed, 1)

            def body(b):
                if valid(b - 2):
                    pool.wait_ge(hid_hi_done, 6 * (b - 2) + 6)
                    for k in (2, 3):
                        split_hidden(hid_a, acts, slice(k, k + 1)).then_inc(hid_lo_pool, 1)
                place_v(b, 3)
                if valid(b + 1):
                    split(b + 1, xT, turned[:], x_hi_done, xT_split)
                if valid(b - 1):
                    split(b - 1, oT, o_chan[:, 0, :], o_hi_done, oT_split)
                if valid(b - 3):
                    inverse_deviation(LN_OUT, b - 3)
                if valid(b + 1):
                    pool.wait_ge(q_hi_done, b + 2)
                    pool_ops.tensor_tensor(q_split[:, 2, :], turned[:], q_split[:, 0, :].bitcast(F32), ALU.subtract).then_inc(q_split_done, 1)
                if valid(b - 3):
                    pool.wait_ge(normed[LN_OUT], 4 * (b - 2))
                    pool_ops.tensor_tensor(y_out[:], y_out[:], x_kept[:], ALU.add).then_inc(out_added, 1)
                if valid(b - 1):
                    inverse_deviation(LN_POST, b - 1)
                    pool.wait_ge(normed[LN_POST], 4 * b)
                    pool.wait_ge(x_res_loaded, 16 * b)
                    wait(pool, x_mid_kept, b - 1)
                    pool_ops.tensor_tensor(x_mid[:], y_post[:], x_res[:], ALU.add).then_inc(x_mid_done, 1)
                if valid(b + 1):
                    pool.wait_ge(k_hi_done, b + 2)
                    pool_ops.tensor_tensor(k_split[:, 1, :], turned[:], k_split[:, 0, :].bitcast(F32), ALU.subtract).then_inc(k_split_done, 1)
                if valid(b - 1):
                    inverse_deviation(LN_MID, b - 1)
                if valid(b - 1):
                    split(b - 1, x2T, turned[:], x2_hi_done, x2T_split)
                place_v(b + 1, 0)
                if valid(b - 1):
                    for o in range(HC - 1):
                        pool.wait_ge(hid_hi_done, 6 * (b - 1) + o + 1)
                        split_hidden(hid_a, gated, slice(o, o + 1)).then_inc(hid_lo_pool, 1)
                place_v(b + 1, 1)
                if valid(b - 2):
                    for half in (0, 1):
                        pool.wait_ge(last_hi_done, 4 * (b - 2) + 2 * half + 2)
                        split_hidden(hid_b, acts, slice(2 * half, 2 * half + 2)).then_inc(last_lo_done, 1)
                if valid(b + 2):
                    inverse_deviation(LN_IN, b + 2)
                place_v(b + 1, 2)

            inverse_deviation(LN_IN, 0)
            iterations(pool, body)


INPUTS = ["L0_attn_x", "L0_attn_qkv_w", "L0_attn_qkv_b", "L0_attn_proj_w", "L0_attn_proj_b", "L0_ffn_w1_w", "L0_ffn_w1_s",
          "L0_ffn_w2_w", "L0_ffn_w2_s", "L0_ffn_h1_w", "L0_ffn_h1_s", "L0_ffn_h2_w", "L0_ffn_h2_s", "L0_ffn_w3_w", "L0_ffn_w3_s"]


def kernel(**inputs):
    import numpy as np
    import concourse.bacc as bacc
    from concourse.bass_utils import run_bass_kernel_spmd

    nc = bacc.Bacc("TRN2", target_bir_lowering=False, num_devices=1)
    arrays, args = {}, []
    for name in INPUTS:
        a = np.ascontiguousarray(inputs[name])
        arrays[f"in_{name}"] = a
        args.append(nc.dram_tensor(f"in_{name}", a.shape, mybir.dt.from_np(a.dtype), kind="ExternalInput").ap())
    args.append(nc.dram_tensor("out_x", (B, N, C), F32, kind="ExternalOutput").ap())
    build(nc, *args)
    r = run_bass_kernel_spmd(nc, [arrays], core_ids=[0])
    return r.results[0]["out_x"]
```
